# Optimizing a Trainium2 kernel written in Bass

```python
import numpy as np
import jax
import jax.numpy as jnp

def _softmax(x, axis=-1):
    return jax.nn.softmax(x, axis=axis)

def _gelu(x):
    return jax.nn.gelu(x, approximate=True)

def _silu(x):
    return jax.nn.silu(x)

def _sigmoid(x):
    return jax.nn.sigmoid(x)

def _layernorm(x, axis=-1, eps=1e-05):
    m = jnp.mean(x, axis=axis, keepdims=True)
    v = jnp.var(x, axis=axis, keepdims=True)
    return (x - m) / jnp.sqrt(v + eps)

def _scatter_add(tgt, idx, src, axis=0):
    return tgt.at[idx].add(src)

def _segment_sum(src, seg, n):
    return jax.ops.segment_sum(src, seg, n)
kernel_name = 'mk_lm_tower_d1_tok_ids1024_r4_90a37d'

def setup_inputs(seed: int=0):
    np.random.seed(seed)
    _w = jnp.asarray

    def _rec_inputs():
        import jax
        import jax.numpy as jnp
        _rk = jax.random.key(seed)
        x = jax.random.randint(jax.random.fold_in(_rk, 1), (4, 2048), 0, 7999, jnp.int32)
        return x
    x = _rec_inputs()

    def _L0_tok_setup():
        import jax, jax.numpy as jnp
        import numpy as np
        VOCAB = 8000
        EMBED = 256
        key = jax.random.key(seed)
        k_ids, k_w = jax.random.split(key)
        token_ids = jax.random.randint(k_ids, (4, 512), 0, VOCAB, dtype=jnp.int64 if jax.config.jax_enable_x64 else jnp.int32)
        weight = jax.random.truncated_normal(k_w, -3.0, 3.0, (VOCAB, EMBED), dtype=jnp.float32)
        return {'token_ids': token_ids, 'weight': weight}
    _L0_tok_all = _L0_tok_setup()
    _L0_tok_in = {k: v for k, v in _L0_tok_all.items() if k in ('weight',)}
    del _L0_tok_all

    def _L0_attn_setup():
        import jax, jax.numpy as jnp
        import numpy as np
        NUM_HEAD = 16
        D_Q = 128
        D_KV = 128
        ROPE_BASE = 10000.0

        def _cos_sin(seq_len, dim):
            pos = jnp.arange(seq_len, dtype=jnp.float32)[:, None]
            ids = jnp.arange(dim // 2, dtype=jnp.float32)
            theta = ROPE_BASE ** (-2.0 * ids) / (dim // 2)
            r = pos * theta[None, :]
            return (jnp.cos(r), jnp.sin(r))

        def _rope(x, cos, sin):
            b, s, d = x.shape
            xv = x.reshape(b, s, d // 2, 2)
            x0, x1 = (xv[..., 0], xv[..., 1])
            out = jnp.stack([x0 * cos - x1 * sin, x1 * cos + x0 * sin], axis=-1)
            return out.reshape(b, s, d)
        key = jax.random.key(seed)
        ks = jax.random.split(key, 10)
        d_model, d_q, d_kv = (256, D_Q, D_KV)
        b, s = (2, 512)
        w = lambda k, i, o: jax.random.normal(k, (i, o), dtype=jnp.float32) * 0.02
        return {'x': jax.random.normal(ks[0], (b, s, d_model), dtype=jnp.float32), 'Wd_q_w': w(ks[1], d_model, d_q), 'Wd_q_b': jnp.zeros((d_q,), jnp.float32), 'Wu_q_w': w(ks[2], d_q, d_model), 'Wu_q_b': jnp.zeros((d_model,), jnp.float32), 'Wq_r_w': w(ks[3], d_q, d_model), 'Wq_r_b': jnp.zeros((d_model,), jnp.float32), 'Wk_r_w': w(ks[4], d_model, d_model), 'Wk_r_b': jnp.zeros((d_model,), jnp.float32), 'Wd_kv_w': w(ks[5], d_model, d_kv), 'Wd_kv_b': jnp.zeros((d_kv,), jnp.float32), 'Wu_k_w': w(ks[6], d_kv, d_model), 'Wu_k_b': jnp.zeros((d_model,), jnp.float32), 'Wu_v_w': w(ks[7], d_kv, d_model), 'Wu_v_b': jnp.zeros((d_model,), jnp.float32), 'Wo_w': w(ks[8], d_model, d_model), 'Wo_b': jnp.zeros((d_model,), jnp.float32)}
    _L0_attn_all = _L0_attn_setup()
    _L0_attn_in = {k: v for k, v in _L0_attn_all.items() if k in ('Wd_q_w', 'Wd_q_b', 'Wu_q_w', 'Wu_q_b', 'Wq_r_w', 'Wq_r_b', 'Wk_r_w', 'Wk_r_b', 'Wd_kv_w', 'Wd_kv_b', 'Wu_k_w', 'Wu_k_b', 'Wu_v_w', 'Wu_v_b', 'Wo_w', 'Wo_b')}
    del _L0_attn_all

    def _L0_ffn_setup():
        import math
        import jax, jax.numpy as jnp
        import numpy as np
        CAPACITY_FACTOR = 1.25
        key = jax.random.key(seed)
        ks = jax.random.split(key, 5)
        B, S, H, F, E = (4, 1024, 256, 256, 32)
        scale_in = 1.0 / math.sqrt(H)
        scale_mid = 1.0 / math.sqrt(F)
        return {'x': jax.random.normal(ks[0], (B, S, H), dtype=jnp.float32), 'w_router': jax.random.normal(ks[1], (H, E), dtype=jnp.float32) * scale_in, 'w_gate': jax.random.normal(ks[2], (E, H, F), dtype=jnp.float32) * scale_in, 'w_up': jax.random.normal(ks[3], (E, H, F), dtype=jnp.float32) * scale_in, 'w_down': jax.random.normal(ks[4], (E, F, H), dtype=jnp.float32) * scale_mid}
    _L0_ffn_all = _L0_ffn_setup()
    _L0_ffn_in = {k: v for k, v in _L0_ffn_all.items() if k in ('w_router', 'w_gate', 'w_up', 'w_down')}
    del _L0_ffn_all
    return {'x': x, 'L0_tok_weight': _L0_tok_in['weight'], 'L0_attn_Wd_q_w': _L0_attn_in['Wd_q_w'], 'L0_attn_Wd_q_b': _L0_attn_in['Wd_q_b'], 'L0_attn_Wu_q_w': _L0_attn_in['Wu_q_w'], 'L0_attn_Wu_q_b': _L0_attn_in['Wu_q_b'], 'L0_attn_Wq_r_w': _L0_attn_in['Wq_r_w'], 'L0_attn_Wq_r_b': _L0_attn_in['Wq_r_b'], 'L0_attn_Wk_r_w': _L0_attn_in['Wk_r_w'], 'L0_attn_Wk_r_b': _L0_attn_in['Wk_r_b'], 'L0_attn_Wd_kv_w': _L0_attn_in['Wd_kv_w'], 'L0_attn_Wd_kv_b': _L0_attn_in['Wd_kv_b'], 'L0_attn_Wu_k_w': _L0_attn_in['Wu_k_w'], 'L0_attn_Wu_k_b': _L0_attn_in['Wu_k_b'], 'L0_attn_Wu_v_w': _L0_attn_in['Wu_v_w'], 'L0_attn_Wu_v_b': _L0_attn_in['Wu_v_b'], 'L0_attn_Wo_w': _L0_attn_in['Wo_w'], 'L0_attn_Wo_b': _L0_attn_in['Wo_b'], 'L0_ffn_w_router': _L0_ffn_in['w_router'], 'L0_ffn_w_gate': _L0_ffn_in['w_gate'], 'L0_ffn_w_up': _L0_ffn_in['w_up'], 'L0_ffn_w_down': _L0_ffn_in['w_down']}

def reference(x, L0_tok_weight, L0_attn_Wd_q_w, L0_attn_Wd_q_b, L0_attn_Wu_q_w, L0_attn_Wu_q_b, L0_attn_Wq_r_w, L0_attn_Wq_r_b, L0_attn_Wk_r_w, L0_attn_Wk_r_b, L0_attn_Wd_kv_w, L0_attn_Wd_kv_b, L0_attn_Wu_k_w, L0_attn_Wu_k_b, L0_attn_Wu_v_w, L0_attn_Wu_v_b, L0_attn_Wo_w, L0_attn_Wo_b, L0_ffn_w_router, L0_ffn_w_gate, L0_ffn_w_up, L0_ffn_w_down):
    import jax
    import jax.numpy as jnp

    def _L0_tok_ref(token_ids, weight):
        import jax, jax.numpy as jnp
        import numpy as np
        VOCAB = 8000
        EMBED = 256
        return jnp.take(weight, token_ids, axis=0)

    def _L0_attn_ref(x, Wd_q_w, Wd_q_b, Wu_q_w, Wu_q_b, Wq_r_w, Wq_r_b, Wk_r_w, Wk_r_b, Wd_kv_w, Wd_kv_b, Wu_k_w, Wu_k_b, Wu_v_w, Wu_v_b, Wo_w, Wo_b):
        import jax, jax.numpy as jnp
        import numpy as np
        NUM_HEAD = 16
        D_Q = 128
        D_KV = 128
        ROPE_BASE = 10000.0

        def _cos_sin(seq_len, dim):
            pos = jnp.arange(seq_len, dtype=jnp.float32)[:, None]
            ids = jnp.arange(dim // 2, dtype=jnp.float32)
            theta = ROPE_BASE ** (-2.0 * ids) / (dim // 2)
            r = pos * theta[None, :]
            return (jnp.cos(r), jnp.sin(r))

        def _rope(x, cos, sin):
            b, s, d = x.shape
            xv = x.reshape(b, s, d // 2, 2)
            x0, x1 = (xv[..., 0], xv[..., 1])
            out = jnp.stack([x0 * cos - x1 * sin, x1 * cos + x0 * sin], axis=-1)
            return out.reshape(b, s, d)
        b, s, d_model = x.shape
        h = NUM_HEAD
        hd = d_model // h
        scale = jnp.sqrt(jnp.float32(h + D_KV + D_Q))

        def heads(t):
            return t.reshape(b, s, h, hd).transpose(0, 2, 1, 3)
        cos, sin = _cos_sin(s, d_model)
        ct_q = x @ Wd_q_w + Wd_q_b
        qt_c = heads(ct_q @ Wu_q_w + Wu_q_b)
        qt_r = heads(_rope(ct_q @ Wq_r_w + Wq_r_b, cos, sin))
        query = qt_c + qt_r
        ct_kv = x @ Wd_kv_w + Wd_kv_b
        kt_c = heads(ct_kv @ Wu_k_w + Wu_k_b)
        kt_r = heads(_rope(x @ Wk_r_w + Wk_r_b, cos, sin))
        key = kt_c + kt_r
        value = heads(ct_kv @ Wu_v_w + Wu_v_b)
        attn = jnp.einsum('bhqd,bhkd->bhqk', query, key) / scale
        attn = jax.nn.softmax(attn, axis=-1)
        out = jnp.einsum('bhqk,bhkd->bhqd', attn, value)
        out = out.transpose(0, 2, 1, 3).reshape(b, s, d_model)
        return out @ Wo_w + Wo_b

    def _L0_ffn_ref(x, w_router, w_gate, w_up, w_down):
        import math
        import jax, jax.numpy as jnp
        import numpy as np
        CAPACITY_FACTOR = 1.25
        B, S, H = x.shape
        E = w_gate.shape[0]
        T = B * S
        C = int(math.ceil(CAPACITY_FACTOR * T / E))
        xt = x.reshape(T, H)
        logits = xt @ w_router
        probs = jax.nn.softmax(logits, axis=-1)
        top1 = jnp.argmax(probs, axis=-1)
        gate = jnp.take_along_axis(probs, top1[:, None], axis=1)[:, 0]
        onehot = jax.nn.one_hot(top1, E, dtype=jnp.int32)
        pos = jnp.cumsum(onehot, axis=0)[jnp.arange(T), top1] - 1
        accepted = pos < C
        slot = jnp.where(accepted, top1 * C + pos, E * C)
        buf = jnp.zeros((E * C + 1, H), dtype=x.dtype).at[slot].set(xt)
        buf = buf[:E * C].reshape(E, C, H)
        g = jnp.einsum('ech,ehf->ecf', buf, w_gate)
        u = jnp.einsum('ech,ehf->ecf', buf, w_up)
        y = jnp.einsum('ecf,efh->ech', jax.nn.silu(g) * u, w_down)
        out_tok = y.reshape(E * C, H)[jnp.clip(slot, 0, E * C - 1)]
        out_tok = jnp.where(accepted[:, None], out_tok * gate[:, None], 0.0)
        return (xt + out_tok).reshape(B, S, H)
    h = _L0_tok_ref(x, L0_tok_weight)
    h = h + _L0_attn_ref(_layernorm(h, axis=-1), L0_attn_Wd_q_w, L0_attn_Wd_q_b, L0_attn_Wu_q_w, L0_attn_Wu_q_b, L0_attn_Wq_r_w, L0_attn_Wq_r_b, L0_attn_Wk_r_w, L0_attn_Wk_r_b, L0_attn_Wd_kv_w, L0_attn_Wd_kv_b, L0_attn_Wu_k_w, L0_attn_Wu_k_b, L0_attn_Wu_v_w, L0_attn_Wu_v_b, L0_attn_Wo_w, L0_attn_Wo_b)
    h = h + _L0_ffn_ref(_layernorm(h, axis=-1), L0_ffn_w_router, L0_ffn_w_gate, L0_ffn_w_up, L0_ffn_w_down)
    return h

_drawn_inputs = setup_inputs


def setup_inputs(seed=0):
    import zlib

    import numpy as np

    out = dict(_drawn_inputs(seed))
    spreads = {'L0_attn_Wd_q_b': (0.0, 0.8),
     'L0_attn_Wu_q_b': (0.0, 0.8),
     'L0_attn_Wq_r_b': (0.0, 0.8),
     'L0_attn_Wk_r_b': (0.0, 2.0),
     'L0_attn_Wd_kv_b': (0.0, 0.8),
     'L0_attn_Wu_k_b': (0.0, 2.0),
     'L0_attn_Wu_v_b': (0.0, 0.341),
     'L0_attn_Wo_b': (0.0, 0.1)}
    factors = {'L0_attn_Wd_q_w': 8.0,
     'L0_attn_Wu_q_w': 8.0,
     'L0_attn_Wq_r_w': 8.0,
     'L0_attn_Wk_r_w': 8.0,
     'L0_attn_Wd_kv_w': 8.0,
     'L0_attn_Wu_k_w': 8.0,
     'L0_attn_Wu_v_w': 6.717}
    for name, (base, spread) in spreads.items():
        noise = np.random.default_rng([zlib.crc32(name.encode()), seed]).standard_normal(out[name].shape)
        drawn = base * np.exp(spread * noise) if base else spread * noise
        out[name] = jnp.asarray(drawn.astype(out[name].dtype))
    for name, factor in factors.items():
        out[name] = (out[name] * factor).astype(out[name].dtype)
    return out
```

```python
from contextlib import ExitStack

import numpy as np

import concourse.bass as bass
from concourse import mybir

F32 = mybir.dt.float32
BF16 = mybir.dt.bfloat16
I32 = mybir.dt.int32
ACT = mybir.ActivationFunctionType
ALU = mybir.AluOpType
AX = mybir.AxisListType

P = 128
BATCH, SEQ, DM = 4, 2048, 256
T = BATCH * SEQ
HEADS, HD = 16, 16
LATENT = 128
EXPERTS, FF = 32, 256
CAP = -(-5 * T // (4 * EXPERTS))
SLOTS = EXPERTS * CAP
EPS = 1e-5
ROPE_BASE = 10000.0
SCALE = float(1.0 / np.sqrt(np.float32(HEADS + LATENT + LATENT)))

CH = 512
CT = CH // P
CPB = SEQ // CH
NCH = T // CH
KD = DM // P
PARTS = 3
PAIRS = [(0, 0), (0, 1), (0, 2), (1, 0), (1, 1), (2, 0)]
SROWS = len(PAIRS) * HD
MROWS = SROWS + PARTS
QUAD = 4
QUADS = BATCH * HEADS // QUAD
VW = 2 * HD
ROW = 2 * DM + 4


def semaphores(nc, ctx):
    taken = []

    def clear():
        nc.clear_and_free_semaphores(taken)
        nc.all_engine_barrier()

    def sem(name):
        taken.append(nc.alloc_semaphore(name))
        return taken[-1]

    ctx.callback(clear)
    return sem


def phase_a(nc, dram, out):
    with ExitStack() as ctx:
        def sb(name, shape, dt=F32):
            return ctx.enter_context(nc.sbuf_tensor(name, shape, dt))

        sem = semaphores(nc, ctx)

        cos_sb = sb("cos_sb", [P, SEQ])
        sin_sb = sb("sin_sb", [P, SEQ])
        ident = sb("ident_a", [P, P])
        w_down = sb("w_down_qkv", [P, 2, KD, LATENT])
        w_uq = sb("w_uq", [LATENT, DM])
        w_qr = sb("w_qr", [LATENT, DM])
        w_uk = sb("w_uk", [LATENT, DM])
        w_kr = sb("w_kr", [P, KD, DM])
        w_uv = sb("w_uv", [LATENT, DM])
        b_cols = sb("b_cols", [P, 10])
        b_v = sb("b_v", [P, DM])
        ids = sb("ids", [P, 4, CT], I32)
        emb = sb("emb", [P, 4, CT, DM])
        stats = sb("stats", [P, 4, CT, 6])
        mv = sb("mv", [P, 4, CT, 2])
        var_eps = sb("var_eps", [P, 4, CT])
        rstd = sb("rstd", [P, 4, CT])
        neg_half = sb("neg_half", [P, CT])
        eps_sb = sb("eps_sb", [P, CT])
        normed = sb("normed", [P, CT, DM])
        normed_t = sb("normed_t", [P, 2, KD, CH])
        lat = sb("lat", [P, 2, 2, CH])
        terms = sb("terms", [P, 2, 4, CH])
        sums = sb("sums", [P, 2, 2, CH])
        full = sb("full", [P, 2, 2, CH])
        rest = sb("rest", [P, 2, 2, CH])
        parts = sb("parts", [P, 2, 2, PARTS, 2, CH], BF16)
        val = sb("val", [P, 2, CT, HEADS, VW])
        ps_t = ctx.enter_context(nc.psum_tensor("ps_t", [P, KD, CH], F32))
        ps_l = ctx.enter_context(nc.psum_tensor("ps_l", [P, 2, CH], F32))
        ps_r = ctx.enter_context(nc.psum_tensor("ps_r", [P, 4, CH], F32))

        ident_in = sem("ident_in_a")
        const_in = sem("const_in")
        tables_in = sem("tables_in")
        ids_in = [sem(f"ids_in{i}") for i in range(4)]
        rows_in = [sem(f"rows_in{i}") for i in range(4)]
        half_set = sem("half_set")
        ones_set = sem("ones_set")
        stats_raw = sem("stats_raw")
        stats_ok = sem("stats_ok")
        eps_ok = sem("eps_ok")
        rstd_ok = sem("rstd_ok")
        norm_ok = sem("norm_ok")
        trans_ok = sem("trans_ok")
        nt_ok = sem("nt_ok")
        lat_ps = sem("lat_ps")
        lat_ok = sem("lat_ok")
        val_ps = sem("val_ps")
        val_ok = sem("val_ok")
        rot_ps = [sem("rot_ps_q"), sem("rot_ps_k")]
        cont_ps = [sem("cont_ps_q"), sem("cont_ps_k")]
        terms_ok = [sem("terms_ok_q"), sem("terms_ok_k")]
        sums_ok = [sem("sums_ok_q"), sem("sums_ok_k")]
        full_ok = [sem("full_ok_q"), sem("full_ok_k")]
        part1_ok = [sem("part1_ok_q"), sem("part1_ok_k")]
        rest_ok = [sem("rest_ok_q"), sem("rest_ok_k")]
        part2_ok = [sem("part2_ok_q"), sem("part2_ok_k")]
        part3_ok = [sem("part3_ok_q"), sem("part3_ok_k")]
        parts_out = [sem("parts_out0"), sem("parts_out1")]
        val_out = [sem("val_out0"), sem("val_out1")]
        emb_out = [sem(f"emb_out{i}") for i in range(4)]

        NCONST = 9
        STORES = 2 * 2 * PARTS

        def after(b, k, n=1):
            return b * (CPB * n) + (k + 1) * n

        def uses(b, k, n, ring=2):
            return b * (CPB // ring * n) + (k // ring) * n

        with nc.Block() as block:
            @block.sync
            def _(sp):
                for i in range(4):
                    sp.dma_start(ids[:, i, :], dram["ids"][i]).then_inc(ids_in[i], 16)
                sp.dma_start(ident[:], dram["ident"]).then_inc(ident_in, 16)
                sp.dma_start(w_down[:, 0], dram["w_dq"].rearrange("(k p) n -> p k n", p=P)).then_inc(const_in, 16)
                sp.dma_start(w_down[:, 1], dram["w_dkv"].rearrange("(k p) n -> p k n", p=P)).then_inc(const_in, 16)
                sp.dma_start(w_kr[:], dram["w_kr"].rearrange("(k p) n -> p k n", p=P)).then_inc(const_in, 16)
                for dst, src in ((b_cols, dram["b_cols"]), (w_qr, dram["w_qr"]), (w_uq, dram["w_uq"]),
                                 (w_uv, dram["w_uv"]), (w_uk, dram["w_uk"]), (b_v, dram["b_v"].to_broadcast([P, DM]))):
                    sp.dma_start(dst[:], src).then_inc(const_in, 16)
                sp.wait_ge(rows_in[0], 16 * CT)
                for dst, src in ((cos_sb, dram["cos"]), (sin_sb, dram["sin"])):
                    sp.dma_start(dst[:], src).then_inc(tables_in, 16)

                def chunk(b, k, last):
                    par = k % 2
                    if not last:
                        sp.wait_ge(rows_in[k], b * (16 * CT) + 16 * CT)
                        nxt = dram["ids"][bass.ds(b * CPB + (k + 4), 1)].rearrange("a p t -> (a p) t")
                        sp.dma_start(ids[:, k, :], nxt).then_inc(ids_in[k], 16)
                    row = b * SEQ + k * CH
                    sp.wait_ge(rows_in[k], b * (16 * CT) + 16 * CT)
                    sp.dma_start(dram["emb"][bass.ds(row, CH)].rearrange("(t p) n -> p t n", p=P), emb[:, k]).then_inc(emb_out[k], 16)
                    sp.wait_ge(val_ok, after(b, k, 2))
                    for t in range(CT):
                        dst = dram["vext"][bass.ds(b * QUAD, QUAD), k * CH + t * P:k * CH + (t + 1) * P, :]
                        sp.dma_start(dst.rearrange("q p n -> p q n"),
                                     val[:, par, t].rearrange("p (q j) n -> p q (j n)", q=QUAD)).then_inc(val_out[par], 16)
                    for x in range(2):
                        sp.wait_ge(part3_ok[x], after(b, k))
                        for g in range(PARTS):
                            for eo in range(2):
                                dst = dram["qk"][x][bass.ds(b * HEADS, HEADS), g, eo, :, k * CH:(k + 1) * CH]
                                sp.dma_start(dst, parts[:, par, x, g, eo, :]).then_inc(parts_out[par], 16)

                with sp.Fori(0, BATCH - 1) as b:
                    for k in range(CPB):
                        chunk(b, k, False)
                for k in range(CPB):
                    chunk(BATCH - 1, k, True)
                for par in range(2):
                    sp.wait_ge(val_out[par], NCH // 2 * CT * 16)
                    sp.wait_ge(parts_out[par], NCH // 2 * STORES * 16)
                for k in range(4):
                    sp.wait_ge(emb_out[k], BATCH * 16)

            @block.gpsimd
            def _(pool):
                def gather(b, k):
                    for t in range(CT):
                        pool.indirect_dma_start(
                            emb[:, k, t, :], None, dram["table"],
                            bass.IndirectOffsetOnAxis(ap=ids[:, k, t:t + 1], axis=0)).then_inc(rows_in[k], 16)

                def root(b, k):
                    pool.wait_ge(stats_ok, after(b, k, CT))
                    pool.tensor_tensor(var_eps[:, k, :], mv[:, k, :, 1], eps_sb[:], ALU.add).then_inc(eps_ok, 1)
                    pool.wait_ge(eps_ok, after(b, k))
                    pool.tensor_tensor(rstd[:, k, :], var_eps[:, k, :], neg_half[:], ALU.pow).then_inc(rstd_ok, 1)

                pool.memset(neg_half[:], -0.5).then_inc(half_set, 1)
                pool.memset(eps_sb[:], EPS).then_inc(half_set, 1)
                pool.wait_ge(half_set, 2)
                for k in range(2):
                    pool.wait_ge(ids_in[k], 16)
                    gather(0, k)
                root(0, 0)
                pool.memset(val[:], 1.0).then_inc(ones_set, 1)
                pool.wait_ge(ids_in[2], 16)
                gather(0, 2)
                root(0, 1)

                def chunk(b, k, last):
                    ahead = None if last and k + 3 >= CPB else (b, k + 3) if k + 3 < CPB else (b + 1, k + 3 - CPB)
                    if ahead:
                        pool.wait_ge(norm_ok, b * (CPB * CT) + k * CT)
                        pool.wait_ge(emb_out[ahead[1]], ahead[0] * 16)
                        pool.wait_ge(ids_in[ahead[1]], ahead[0] * 16 + 16)
                    pool.wait_ge(terms_ok[0], after(b, k, 4))
                    pool.wait_ge(full_ok[0], b * (CPB * 2) + k * 2)
                    pool.tensor_tensor(sums[:, 0, 0, :], terms[:, 0, 0, :], terms[:, 0, 1, :], ALU.subtract).then_inc(sums_ok[0], 1)
                    pool.tensor_tensor(sums[:, 0, 1, :], terms[:, 0, 2, :], terms[:, 0, 3, :], ALU.add).then_inc(sums_ok[0], 1)
                    if ahead:
                        gather(*ahead)
                    for x in range(2):
                        pool.wait_ge(part1_ok[x], after(b, k))
                        pool.wait_ge(part3_ok[x], b * CPB + k)
                        pool.tensor_tensor(rest[:, x], full[:, x], parts[:, k % 2, x, 0], ALU.subtract).then_inc(rest_ok[x], 1)
                    if not (last and k + 2 >= CPB):
                        root(*((b, k + 2) if k + 2 < CPB else (b + 1, k + 2 - CPB)))

                with pool.Fori(0, BATCH - 1) as b:
                    for k in range(CPB):
                        chunk(b, k, False)
                for k in range(CPB):
                    chunk(BATCH - 1, k, True)

            @block.tensor
            def _(pe):
                def transpose(b, k):
                    pe.wait_ge(norm_ok, after(b, k, CT))
                    pe.wait_ge(nt_ok, b * CPB + k)
                    for t in range(CT):
                        for d in range(KD):
                            last = pe.transpose(ps_t[:, d, t * P:(t + 1) * P], normed[:, t, d * P:(d + 1) * P], ident[:])
                    last.then_inc(trans_ok, 1)

                def latent(b, k):
                    pe.wait_ge(nt_ok, after(b, k))
                    for x in range(2):
                        for d in range(KD):
                            last = pe.matmul(ps_l[:, x, :], w_down[:, x, d, :], normed_t[:, k % 2, d, :],
                                             start=d == 0, stop=d == KD - 1)
                        last.then_inc(lat_ps, 1)

                def rotary(b, k, x):
                    if x == 0:
                        pe.wait_ge(terms_ok[1], b * (CPB * 4) + k * 4)
                        pe.wait_ge(lat_ok, after(b, k, 2))
                    else:
                        pe.wait_ge(terms_ok[0], after(b, k, 4))
                    for eo in range(2):
                        cols = slice(eo * P, (eo + 1) * P)
                        if x == 0:
                            last = pe.matmul(ps_r[:, eo, :], w_qr[:, cols], lat[:, k % 2, 0, :], start=True, stop=True)
                        else:
                            for d in range(KD):
                                last = pe.matmul(ps_r[:, eo, :], w_kr[:, d, cols], normed_t[:, k % 2, d, :],
                                                 start=d == 0, stop=d == KD - 1)
                    last.then_inc(rot_ps[x], 1)

                def content(b, k, x):
                    pe.wait_ge(full_ok[1 - x], after(b, k, 2) if x else b * (CPB * 2) + k * 2)
                    w = (w_uq, w_uk)[x]
                    for eo in range(2):
                        last = pe.matmul(ps_r[:, 2 + eo, :], w[:, eo * P:(eo + 1) * P], lat[:, k % 2, x, :], start=True, stop=True)
                    last.then_inc(cont_ps[x], 1)

                def values(b, k):
                    for t in range(CT):
                        last = pe.matmul(ps_l[:, t // 2, (t % 2) * DM:(t % 2 + 1) * DM],
                                         lat[:, k % 2, 1, t * P:(t + 1) * P], w_uv[:], start=True, stop=True)
                        if t % 2:
                            last.then_inc(val_ps, 1)

                pe.wait_ge(ident_in, 16)
                transpose(0, 0)
                pe.wait_ge(const_in, 16 * NCONST)
                latent(0, 0)

                def chunk(b, k, last):
                    more = not (last and k == CPB - 1)
                    nxt = (b, k + 1) if k + 1 < CPB else (b + 1, 0)
                    rotary(b, k, 0)
                    content(b, k, 0)
                    values(b, k)
                    if more:
                        transpose(*nxt)
                    rotary(b, k, 1)
                    if more:
                        pe.wait_ge(val_ok, after(b, k, 2))
                        latent(*nxt)
                    content(b, k, 1)

                with pe.Fori(0, BATCH - 1) as b:
                    for k in range(CPB):
                        chunk(b, k, False)
                for k in range(CPB):
                    chunk(BATCH - 1, k, True)

            @block.scalar
            def _(act):
                def copy_nt(b, k):
                    act.wait_ge(trans_ok, after(b, k))
                    act.activation(normed_t[:, k % 2], ps_t[:], ACT.Copy).then_inc(nt_ok, 1)

                def copy_lat(b, k):
                    for x in range(2):
                        act.wait_ge(lat_ps, after(b, k, 2) - (1 - x))
                        act.activation(lat[:, k % 2, x, :], ps_l[:, x, :], ACT.Identity,
                                       bias=b_cols[:, x:x + 1]).then_inc(lat_ok, 1)

                copy_nt(0, 0)
                act.wait_ge(const_in, 16 * NCONST)
                copy_lat(0, 0)

                def split(b, k, x):
                    act.wait_ge(full_ok[x], after(b, k, 2))
                    act.wait_ge(parts_out[k % 2], uses(b, k, STORES * 16))
                    act.activation(parts[:, k % 2, x, 0], full[:, x], ACT.Copy).then_inc(part1_ok[x], 1)
                    act.wait_ge(rest_ok[x], after(b, k))
                    act.activation(parts[:, k % 2, x, 1], rest[:, x], ACT.Copy).then_inc(part2_ok[x], 1)

                def chunk(b, k, last):
                    more = not (last and k == CPB - 1)
                    nxt = (b, k + 1) if k + 1 < CPB else (b + 1, 0)
                    if more:
                        copy_nt(*nxt)
                    split(b, k, 0)
                    if more:
                        copy_lat(*nxt)
                    split(b, k, 1)

                with act.Fori(0, BATCH - 1) as b:
                    for k in range(CPB):
                        chunk(b, k, False)
                for k in range(CPB):
                    chunk(BATCH - 1, k, True)

            @block.vector
            def _(dve):
                def row_stats(b, k):
                    dve.wait_ge(rows_in[k], b * (16 * CT) + 16 * CT)
                    for t in range(CT):
                        dve.bn_stats(stats[:, k, t, :], emb[:, k, t, :]).then_inc(stats_raw, 1)

                def row_moments(b, k):
                    for t in range(CT):
                        dve.bn_aggr(mv[:, k, t, :], stats[:, k, t, :]).then_inc(stats_ok, 1)

                def normalise(b, k):
                    dve.wait_ge(rstd_ok, after(b, k))
                    dve.wait_ge(trans_ok, b * CPB + k)
                    for t in range(CT):
                        dve.tensor_scalar(normed[:, t, :], emb[:, k, t, :], mv[:, k, t, 0:1], rstd[:, k, t:t + 1],
                                          ALU.subtract, ALU.mult).then_inc(norm_ok, 1)

                def rope_terms(b, k, x):
                    pos = slice(k * CH, (k + 1) * CH)
                    dve.wait_ge(rot_ps[x], after(b, k))
                    if x == 0:
                        dve.wait_ge(sums_ok[0], b * (CPB * 2) + k * 2)
                    for n, (eo, tab) in enumerate(((0, cos_sb), (1, sin_sb), (1, cos_sb), (0, sin_sb))):
                        dve.scalar_tensor_tensor(terms[:, x, n, :], ps_r[:, eo, :], b_cols[:, 2 + 4 * x + eo:3 + 4 * x + eo],
                                                 tab[:, pos], ALU.add, ALU.mult).then_inc(terms_ok[x], 1)

                def add_content(b, k, x):
                    dve.wait_ge(cont_ps[x], after(b, k))
                    dve.wait_ge(sums_ok[x], after(b, k, 2))
                    dve.wait_ge(rest_ok[x], b * CPB + k)
                    for eo in range(2):
                        dve.scalar_tensor_tensor(full[:, x, eo, :], ps_r[:, 2 + eo, :], b_cols[:, 4 + 4 * x + eo:5 + 4 * x + eo],
                                                 sums[:, x, eo, :], ALU.add, ALU.add).then_inc(full_ok[x], 1)

                def third(b, k, x):
                    dve.wait_ge(part2_ok[x], after(b, k))
                    dve.tensor_tensor(parts[:, k % 2, x, 2], rest[:, x], parts[:, k % 2, x, 1],
                                      ALU.subtract).then_inc(part3_ok[x], 1)

                row_stats(0, 0)
                dve.wait_ge(stats_raw, CT)
                row_moments(0, 0)
                normalise(0, 0)
                row_stats(0, 1)
                dve.wait_ge(stats_raw, 2 * CT)
                row_moments(0, 1)
                dve.wait_ge(const_in, 16 * NCONST)
                dve.wait_ge(tables_in, 32)
                dve.wait_ge(ones_set, 1)

                def chunk(b, k, first, last):
                    rope_terms(b, k, 0)
                    if not (last and k == CPB - 1):
                        normalise(*((b, k + 1) if k + 1 < CPB else (b + 1, 0)))
                    if not (first and k == 0):
                        third(*((b, k - 1) if k else (b - 1, CPB - 1)), 1)
                    add_content(b, k, 0)
                    dve.wait_ge(val_out[k % 2], uses(b, k, CT * 16))
                    for h in range(2):
                        dve.wait_ge(val_ps, after(b, k, 2) - (1 - h))
                        dve.tensor_tensor(val[:, k % 2, 2 * h:2 * h + 2, :, 0:HD],
                                          ps_l[:, h, :].rearrange("p (t h d) -> p t h d", t=2, d=HD),
                                          bv_twice, ALU.add).then_inc(val_ok, 1)
                    ahead = None if last and k + 2 >= CPB else (b, k + 2) if k + 2 < CPB else (b + 1, k + 2 - CPB)
                    if ahead:
                        row_stats(*ahead)
                        dve.wait_ge(stats_raw, after(*ahead, CT))
                    rope_terms(b, k, 1)
                    if ahead:
                        row_moments(*ahead)
                    dve.wait_ge(terms_ok[1], after(b, k, 4))
                    dve.tensor_tensor(sums[:, 1, 0, :], terms[:, 1, 0, :], terms[:, 1, 1, :], ALU.subtract).then_inc(sums_ok[1], 1)
                    dve.tensor_tensor(sums[:, 1, 1, :], terms[:, 1, 2, :], terms[:, 1, 3, :], ALU.add).then_inc(sums_ok[1], 1)
                    third(b, k, 0)
                    add_content(b, k, 1)

                bv_twice = b_v[:].rearrange("p (a h d) -> p a h d", a=1, d=HD).to_broadcast([P, 2, HEADS, HD])
                for k in range(CPB):
                    chunk(0, k, True, False)
                with dve.Fori(1, BATCH - 1) as b:
                    for k in range(CPB):
                        chunk(b, k, False, False)
                for k in range(CPB):
                    chunk(BATCH - 1, k, False, True)
                third(BATCH - 1, CPB - 1, 1)


def phase_b(nc, dram, out):
    UNITS = 2 * (SEQ // CH)
    KT = SEQ // P
    TILES = UNITS * KT * QUAD
    PER_UNIT = KT * QUAD
    STEPS = QUADS // 2
    LEAD = PER_UNIT + 16
    BANKS = 3
    RING = 16
    SLOTS_PV = RING // QUAD
    QT = CH // P
    KC = SEQ // 512

    with ExitStack() as ctx:
        def sb(name, shape, dt=F32):
            return ctx.enter_context(nc.sbuf_tensor(name, shape, dt))

        sem = semaphores(nc, ctx)

        keys = sb("keys", [P, 2, QUAD, SEQ], BF16)
        queries = sb("queries", [P, 2, SEQ // CH, QUAD, CH], BF16)
        vals = sb("vals", [P, 2, KT, QUAD * VW])
        probs = sb("probs", [P, RING, CH])
        max_parts = sb("max_parts", [P, 2, PER_UNIT])
        neg_max = sb("neg_max", [P, 2, QUAD * QT])
        neg_rest = sb("neg_rest", [P, 2, 2, QUAD * QT])
        neg_split = sb("neg_split", [P, 2, PARTS, QUAD * QT], BF16)
        neg_rows = sb("neg_rows", [PARTS * QUAD * QT, 2, P], BF16)
        ident = sb("ident_b", [P, P], BF16)
        ident_f = sb("ident_bf", [P, P])
        zeros = sb("zeros_b", [P, QUAD * QT])
        weighted = sb("weighted", [P, 2, CH])
        denom = sb("denom", [P, 2, QUAD * CH // P])
        recip = sb("recip", [P, 2, QUAD * CH // P])
        recip_rows = sb("recip_rows", [P, 2, CH])
        heads_out = sb("heads_out", [P, 2, CH])
        ps_s = [ctx.enter_context(nc.psum_tensor(f"ps_s{i}", [P, CH], F32)) for i in range(BANKS)]
        ps_m = [ctx.enter_context(nc.psum_tensor(f"ps_m{i}", [P, CH], F32)) for i in range(BANKS)]
        ps_o = ctx.enter_context(nc.psum_tensor("ps_o", [P, CH], F32))
        ps_n = ctx.enter_context(nc.psum_tensor("ps_n", [P, 1024], BF16))

        ident_in = sem("ident_in")
        ident_ok = sem("ident_ok")
        ones_ok = sem("ones_ok")
        stacks_in = [sem("stacks_in0"), sem("stacks_in1")]
        vals_in = [sem("vals_in0"), sem("vals_in1")]
        early_in = sem("early_in")
        scores_ok = sem("scores_ok")
        probs_ok = [sem(f"probs_ok{i}") for i in range(BANKS)]
        maxima_ps = sem("maxima_ps")
        maxima_ok = [sem(f"maxima_ok{i}") for i in range(BANKS)]
        neg_ok = sem("neg_ok")
        neg_1 = sem("neg_1")
        neg_r1 = sem("neg_r1")
        neg_2 = sem("neg_2")
        neg_r2 = sem("neg_r2")
        split_ok = sem("split_ok")
        rows_ps = sem("rows_ps")
        rows_ok = sem("rows_ok")
        rows_in = [sem("max_rows_in0"), sem("max_rows_in1")]
        pv_ok = [sem(f"pv_ok{i}") for i in range(SLOTS_PV)]
        weighted_ok = sem("weighted_ok")
        denom_in = [sem("denom_in0"), sem("denom_in1")]
        recip_ok = sem("recip_ok")
        recip_out = [sem("recip_out0"), sem("recip_out1")]
        recip_in = [sem("recip_in0"), sem("recip_in1")]
        heads_ok = sem("heads_ok")
        heads_out_done = [sem("heads_out_done0"), sem("heads_out_done1")]

        LOADS = (3 + len(PAIRS) * SEQ // CH) * 16
        EARLY = (3 + len(PAIRS)) * 16

        def total(ring):
            return [len(range(i, TILES, ring)) for i in range(ring)]

        per_bank = total(BANKS)
        lead_uses = [len(range(i, LEAD, BANKS)) for i in range(BANKS)]

        with nc.Block() as block:
            @block.sync
            def _(sp):
                def load_keys(quad, par, done):
                    src = dram["qk"][1][bass.ds(quad * QUAD, QUAD)].rearrange("j g e i t -> (g e i) j t")
                    row = 0
                    for n in (3, 2, 1):
                        sp.dma_start(keys[row:row + n * HD, par], src[0:n * HD]).then_inc(done, 16)
                        row += n * HD

                def load_queries(quad, par, qt, done):
                    src = dram["qk"][0][bass.ds(quad * QUAD, QUAD)].rearrange("j g e i t -> (g e i) j t")
                    for row, (part, _) in enumerate(PAIRS):
                        sp.dma_start(queries[row * HD:(row + 1) * HD, par, qt],
                                     src[part * HD:(part + 1) * HD, :, qt * CH:(qt + 1) * CH]).then_inc(done, 16)

                def load_stacks(quad, par):
                    load_keys(quad, par, stacks_in[par])
                    for qt in range(SEQ // CH):
                        load_queries(quad, par, qt, stacks_in[par])

                def load_vals(quad, par):
                    for half in range(2):
                        src = dram["vext"][bass.ds(quad, 1), half * (SEQ // 2):(half + 1) * (SEQ // 2)]
                        sp.dma_start(vals[:, par, half * (KT // 2):(half + 1) * (KT // 2)],
                                     src.rearrange("q (k p) n -> (q p) k n", p=P)).then_inc(vals_in[par], 16)

                def max_rows(step, lu):
                    par, qt = (lu // 4) % 2, lu % 4
                    sp.wait_ge(rows_ok, step * UNITS + lu + 1)
                    for r in range(PARTS):
                        dst = queries[SROWS + r:SROWS + r + 1, par, qt].rearrange("p j (t q) -> p (j t) q", q=P)
                        sp.dma_start(dst, neg_rows[r * QUAD * QT:(r + 1) * QUAD * QT, lu % 2, :]).then_inc(rows_in[lu % 2], 16)

                def finish(step, lu):
                    sp.wait_ge(weighted_ok, step * UNITS + lu + 1)
                    for j in range(QUAD):
                        row = VW * j + HD
                        sp.dma_start(denom[32 * j:32 * j + 32, lu % 2, :], weighted[row:row + 1, lu % 2, :].rearrange("a (p c) -> a p c", p=32)).then_inc(denom_in[lu % 2], 16)
                    sp.wait_ge(recip_ok, step * UNITS + lu + 1)
                    scratch = dram["recip"][lu % 2]
                    sp.dma_start(scratch.rearrange("j (p c) -> (j p) c", p=32), recip[:, lu % 2, :]).then_inc(recip_out[lu % 2], 16)
                    sp.wait_ge(recip_out[lu % 2], step * (UNITS // 2 * 16) + (lu // 2) * 16 + 16)
                    rows = scratch.rearrange("j (a t) -> j a t", a=1).to_broadcast([QUAD, VW, CH])
                    sp.dma_start(recip_rows[:, lu % 2, :], rows).then_inc(recip_in[lu % 2], 16)
                    sp.wait_ge(heads_ok, step * UNITS + lu + 1)
                    dst = dram["att"][bass.ds((step * 2 + lu // 4) * QUAD, QUAD), :, (lu % 4) * CH:(lu % 4 + 1) * CH]
                    sp.dma_start(dst.rearrange("a d t -> (a d) t"), heads_out[:, lu % 2, :]).then_inc(heads_out_done[lu % 2], 16)

                sp.dma_start(ident_f[:], dram["ident"]).then_inc(ident_in, 16)
                load_keys(0, 0, early_in)
                load_queries(0, 0, 0, early_in)
                for qt in range(1, SEQ // CH):
                    load_queries(0, 0, qt, stacks_in[0])
                load_vals(0, 0)
                max_rows(0, 0)

                def step_of(step, first, last):
                    for lu in range(UNITS):
                        q = lu // 4
                        if not (first and lu == 0):
                            finish(*((step, lu - 1) if lu else (step - 1, UNITS - 1)))
                        if lu % 4 == 0 and not (last and q == 1):
                            if not (first and q == 0):
                                sp.wait_ge(weighted_ok, step * UNITS + lu)
                            load_stacks(step * 2 + (q + 1), 1 - q)
                        if lu % 4 == 1 and not (last and q == 1):
                            load_vals(step * 2 + (q + 1), 1 - q)
                        if not (last and lu == UNITS - 1):
                            max_rows(step, lu + 1)

                step_of(0, True, False)
                with sp.Fori(1, STEPS - 1) as step:
                    step_of(step, False, False)
                step_of(STEPS - 1, False, True)
                finish(STEPS - 1, UNITS - 1)
                for i in range(2):
                    sp.wait_ge(heads_out_done[i], STEPS * UNITS // 2 * 16)

            @block.gpsimd
            def _(pool):
                pool.memset(zeros[:], 0.0).then_inc(ones_ok, 1)
                pool.wait_ge(ones_ok, 1)
                pool.memset(keys[SROWS:MROWS], 1.0).then_inc(ones_ok, 1)
                pool.wait_ge(ones_ok, 2)

                def split(step, lu):
                    par, n = lu % 2, step * UNITS + lu + 1
                    pool.wait_ge(neg_ok, n)
                    pool.tensor_tensor(neg_split[:, par, 0], neg_max[:, par], zeros[:], ALU.add).then_inc(neg_1, 1)
                    pool.wait_ge(neg_1, n)
                    pool.tensor_tensor(neg_rest[:, par, 0], neg_max[:, par], neg_split[:, par, 0], ALU.subtract).then_inc(neg_r1, 1)
                    pool.wait_ge(neg_r1, n)
                    pool.tensor_tensor(neg_split[:, par, 1], neg_rest[:, par, 0], zeros[:], ALU.add).then_inc(neg_2, 1)
                    pool.wait_ge(neg_2, n)
                    pool.tensor_tensor(neg_split[:, par, 2], neg_rest[:, par, 0], neg_split[:, par, 1], ALU.subtract).then_inc(split_ok, 1)

                def normalise(step, lu):
                    pool.wait_ge(recip_in[lu % 2], step * (UNITS // 2 * 16) + (lu // 2) * 16 + 16)
                    pool.wait_ge(heads_out_done[lu % 2], step * (UNITS // 2 * 16) + (lu // 2) * 16)
                    pool.tensor_tensor(heads_out[:, lu % 2, :], weighted[:, lu % 2, :], recip_rows[:, lu % 2, :], ALU.mult).then_inc(heads_ok, 1)

                def step_of(step, first, last):
                    for lu in range(UNITS):
                        if not (first and lu == 0):
                            normalise(*((step, lu - 1) if lu else (step - 1, UNITS - 1)))
                        if not (last and lu == UNITS - 1):
                            split(step, lu + 1)

                split(0, 0)
                step_of(0, True, False)
                with pool.Fori(1, STEPS - 1) as step:
                    step_of(step, False, False)
                step_of(STEPS - 1, False, True)
                normalise(STEPS - 1, UNITS - 1)

            @block.tensor
            def _(pe):
                def maximum(step, n):
                    m = n + LEAD
                    lu, g = m // PER_UNIT, m % PER_UNIT
                    par, qt = (lu // 4) % 2, lu % 4
                    j, t, c = g // (QT * KC), g // KC % QT, g % KC
                    if n < 0:
                        bank, used = m % BANKS, m // BANKS
                    else:
                        bank, used = n % BANKS, step * per_bank[n % BANKS] + (lead_uses[n % BANKS] + n // BANKS)
                    if not (n < 0 and m < BANKS):
                        pe.wait_ge(maxima_ok[bank], used)
                    if g == 0 and qt == 0:
                        if n == -LEAD:
                            pe.wait_ge(early_in, EARLY)
                        else:
                            pe.wait_ge(stacks_in[par], step * LOADS + (lu // 8 + 1) * LOADS - (0 if par else EARLY))
                    if n == PER_UNIT - LEAD:
                        pe.wait_ge(stacks_in[0], LOADS - EARLY)
                    pe.matmul(ps_m[bank][:], queries[0:SROWS, par, qt, j, t * P:(t + 1) * P],
                              keys[0:SROWS, par, j, c * 512:(c + 1) * 512], start=True, stop=True).then_inc(maxima_ps, 1)

                def may_turn(step, lu):
                    pe.wait_ge(split_ok, step * UNITS + lu + 1)
                    pe.wait_ge(rows_ok, step * UNITS + lu)

                def turn(step, lu):
                    pe.transpose(ps_n[0:PARTS * QUAD * QT, 0:P], neg_split[:, lu % 2].rearrange("p a b -> p (a b)"), ident[:]).then_inc(rows_ps, 1)

                def scores(step, n):
                    lu, k, j = n // PER_UNIT, n // QUAD % KT, n % QUAD
                    par, qt = (lu // 4) % 2, lu % 4
                    pe.wait_ge(probs_ok[n % BANKS], step * per_bank[n % BANKS] + n // BANKS)
                    if n % PER_UNIT == 0:
                        pe.wait_ge(rows_in[lu % 2], step * (UNITS // 2 * PARTS * 16) + (lu // 2 + 1) * PARTS * 16)
                    pe.matmul(ps_s[n % BANKS][:], keys[0:MROWS, par, j, k * P:(k + 1) * P],
                              queries[0:MROWS, par, qt, j, :], start=True, stop=True).then_inc(scores_ok, 1)

                def weigh(step, n):
                    lu, k = n // PER_UNIT, n // QUAD % KT
                    par = (lu // 4) % 2
                    last_tile = n + QUAD - 1
                    pe.wait_ge(probs_ok[last_tile % BANKS], step * per_bank[last_tile % BANKS] + last_tile // BANKS + 1)
                    if k == 0:
                        pe.wait_ge(weighted_ok, step * UNITS + lu)
                        if lu % 4 == 0:
                            pe.wait_ge(vals_in[par], step * 32 + 32)
                    for j in range(QUAD):
                        mm = pe.matmul(ps_o[32 * j:32 * j + 32, :], vals[:, par, k, VW * j:VW * (j + 1)],
                                       probs[:, (n + j) % RING, :], start=k == 0, stop=k == KT - 1)
                    mm.then_inc(pv_ok[n // QUAD % SLOTS_PV], 1)

                pe.wait_ge(ident_ok, 1)
                for n in range(-LEAD, 0):
                    maximum(0, n)
                    if n == PER_UNIT - LEAD + 8:
                        may_turn(0, 0)
                        turn(0, 0)
                pe.wait_ge(ones_ok, 2)

                def step_of(step, first, last):
                    for n in range(0, TILES, QUAD):
                        lu, k = n // PER_UNIT, n // QUAD % KT
                        turns = k == 14 and not (last and lu == UNITS - 1)
                        if turns:
                            may_turn(step, lu + 1)
                        for i in range(QUAD):
                            scores(step, n + i)
                            if turns and i == 0:
                                turn(step, lu + 1)
                            if not (last and n + i + LEAD >= TILES):
                                maximum(step, n + i)
                        if n:
                            weigh(step, n - QUAD)
                        elif not first:
                            weigh(step - 1, TILES - QUAD)

                step_of(0, True, False)
                with pe.Fori(1, STEPS - 1) as step:
                    step_of(step, False, False)
                step_of(STEPS - 1, False, True)
                weigh(STEPS - 1, TILES - QUAD)

            @block.scalar
            def _(act):
                def copy_rows(step, lu):
                    act.wait_ge(rows_ps, step * UNITS + lu + 1)
                    act.wait_ge(rows_in[lu % 2], step * (UNITS // 2 * PARTS * 16) + (lu // 2) * PARTS * 16)
                    act.activation(neg_rows[:, lu % 2, :], ps_n[0:PARTS * QUAD * QT, 0:P], ACT.Copy).then_inc(rows_ok, 1)

                def copy_weighted(step, lu):
                    act.wait_ge(pv_ok[SLOTS_PV - 1], step * (TILES // RING) + (lu + 1) * (PER_UNIT // RING))
                    act.wait_ge(heads_ok, step * UNITS + lu - 1) if not (isinstance(step, int) and step == 0 and lu < 2) else None
                    act.activation(weighted[:, lu % 2, :], ps_o[:], ACT.Copy).then_inc(weighted_ok, 1)

                copy_rows(0, 0)

                def step_of(step, first, last):
                    for n in range(TILES):
                        lu, k, j = n // PER_UNIT, n // QUAD % KT, n % QUAD
                        act.wait_ge(scores_ok, step * TILES + n + 1)
                        if j == 0:
                            act.wait_ge(pv_ok[n // QUAD % SLOTS_PV], step * (TILES // RING) + n // RING)
                        act.activation(probs[:, n % RING, :], ps_s[n % BANKS][:], ACT.Exp, scale=SCALE).then_inc(probs_ok[n % BANKS], 1)
                        if k == 14 and j == 0 and not (last and lu == UNITS - 1):
                            copy_rows(step, lu + 1)
                        if k == 1 and j == 0:
                            if lu:
                                copy_weighted(step, lu - 1)
                            elif not first:
                                copy_weighted(step - 1, UNITS - 1)

                step_of(0, True, False)
                with act.Fori(1, STEPS - 1) as step:
                    step_of(step, False, False)
                step_of(STEPS - 1, False, True)
                copy_weighted(STEPS - 1, UNITS - 1)

            @block.vector
            def _(dve):
                def reduce_max(step, n):
                    m = n + LEAD
                    lu, g = m // PER_UNIT, m % PER_UNIT
                    bank = (m if n < 0 else n) % BANKS
                    dve.wait_ge(maxima_ps, step * TILES + m + 1)
                    dve.tensor_reduce(max_parts[:, lu % 2, g:g + 1], ps_m[bank][:], AX.X, ALU.max).then_inc(maxima_ok[bank], 1)
                    if g == PER_UNIT - 1:
                        used = lead_uses[bank] if n >= 0 else 0
                        base = (m if n < 0 else n) // BANKS + 1 + used
                        dve.wait_ge(maxima_ok[bank], step * per_bank[bank] + base)
                        if not (isinstance(step, int) and step * UNITS + lu < 2):
                            dve.wait_ge(split_ok, step * UNITS + lu - 1)
                        dve.tensor_reduce(neg_max[:, lu % 2, :], max_parts[:, lu % 2, :].rearrange("p (a c) -> p a c", c=KC),
                                          AX.X, ALU.max, negate=True).then_inc(neg_ok, 1)

                def reciprocals(step, lu):
                    dve.wait_ge(denom_in[lu % 2], step * (UNITS // 2 * QUAD * 16) + (lu // 2 + 1) * QUAD * 16)
                    dve.wait_ge(recip_out[lu % 2], step * (UNITS // 2 * 16) + (lu // 2) * 16)
                    dve.reciprocal(recip[:, lu % 2, :], denom[:, lu % 2, :]).then_inc(recip_ok, 1)

                dve.wait_ge(ident_in, 16)
                dve.tensor_copy(ident[:], ident_f[:]).then_inc(ident_ok, 1)
                for n in range(-LEAD, 0):
                    reduce_max(0, n)

                def step_of(step, first, last):
                    for n in range(TILES):
                        lu, k, j = n // PER_UNIT, n // QUAD % KT, n % QUAD
                        prev = None if first and lu == 0 else (step, lu - 1) if lu else (step - 1, UNITS - 1)
                        if not (last and n + LEAD >= TILES):
                            reduce_max(step, n)
                        if prev and k == 5 and j == 0:
                            reciprocals(*prev)

                step_of(0, True, False)
                with dve.Fori(1, STEPS - 1) as step:
                    step_of(step, False, False)
                step_of(STEPS - 1, False, True)
                reciprocals(STEPS - 1, UNITS - 1)


EXPERT_RING = 4


class ExpertWeights:

    def __init__(self, nc, ctx):
        shape = [P, EXPERT_RING, 2 * KD, FF]
        self.gate = ctx.enter_context(nc.sbuf_tensor("w_gate", shape, F32))
        self.up = ctx.enter_context(nc.sbuf_tensor("w_up", shape, F32))
        self.down = ctx.enter_context(nc.sbuf_tensor("w_down", [P, EXPERT_RING, 2 * FF // P, DM], F32))
        sem = semaphores(nc, ctx)
        self.gate_up_in = [sem(f"gate_up_in{i}") for i in range(EXPERT_RING)]
        self.down_in = [sem(f"down_in{i}") for i in range(EXPERT_RING)]

    def load(self, sp, dram, s, k):
        e = s * (2 * EXPERT_RING) + 2 * k
        for dst, name, done in ((self.gate, "w_gate", self.gate_up_in), (self.up, "w_up", self.gate_up_in), (self.down, "w_down", self.down_in)):
            src = dram[name][bass.ds(e, 2)].rearrange("e (d p) f -> p (e d) f", p=P)
            for h in range(2):
                sp.dma_start(dst[:, k, 2 * h:2 * h + 2], src[:, 2 * h:2 * h + 2]).then_inc(done[k], 16)


def phase_c(nc, dram, out, experts):
    NCONST = 6
    FAR = float(1 << 20)

    with ExitStack() as ctx:
        def sb(name, shape, dt=F32):
            return ctx.enter_context(nc.sbuf_tensor(name, shape, dt))

        sem = semaphores(nc, ctx)

        ident = sb("ident_c", [P, P])
        tri_f = sb("tri_f", [P, P])
        earlier = sb("earlier", [P, P], BF16)
        all_ones = sb("all_ones", [P, P], BF16)
        w_o = sb("w_o", [P, KD, DM])
        w_router = sb("w_router", [P, KD, EXPERTS])
        b_o = sb("b_o", [P, DM])
        expert_no = sb("expert_no", [P, CT, EXPERTS])
        no_token = sb("no_token", [P, SLOTS // P], I32)
        att_t = sb("att_t", [P, 2, KD, CH])
        emb = sb("emb_c", [P, CPB, CT, DM])
        token_no = sb("token_no", [P, CPB, CT], I32)
        emb_bias = sb("emb_bias", [P, 2, CT, DM])
        resid = sb("resid", [P, 2, CT, DM])
        stats = sb("stats_c", [P, CT, 6])
        mv = sb("mv_c", [P, 2, CT, 2])
        var_eps = sb("var_eps_c", [P, 2, CT])
        rstd = sb("rstd_c", [P, 2, CT])
        neg_half = sb("neg_half_c", [P, CT])
        eps_sb = sb("eps_c", [P, CT])
        rows = sb("rows_c", [P, CPB, CT, ROW])
        rows_t = sb("rows_t", [P, 2, KD, CH])
        top = sb("top", [P, 2, CT])
        is_top = sb("is_top", [P, 2, CT, EXPERTS])
        below_top = sb("below_top", [P, 2, CT, EXPERTS])
        expd = sb("expd", [P, 2, CT, EXPERTS])
        marked = sb("marked", [P, 2, CT, EXPERTS])
        choice = sb("choice", [P, 2, CT])
        onehot = sb("onehot", [P, 2, CT, EXPERTS], BF16)
        exp_sum = sb("exp_sum", [P, 2, CT])
        carry = sb("carry", [P, 2, EXPERTS])
        places = sb("places", [P, 2, CT, EXPERTS])
        own_place = sb("own_place", [P, 2, CT, EXPERTS])
        place = sb("place", [P, 2, CT])
        over = sb("over", [P, 2, CT])
        slot_near = sb("slot_near", [P, 2, CT])
        slot = sb("slot", [P, CPB, CT], I32)
        ps_p = ctx.enter_context(nc.psum_tensor("ps_p", [P, 2, CH], F32))
        ps_t = ctx.enter_context(nc.psum_tensor("ps_tc", [P, KD, CH], F32))
        ps_l = ctx.enter_context(nc.psum_tensor("ps_lc", [P, CT, EXPERTS], F32))
        ps_c = ctx.enter_context(nc.psum_tensor("ps_c", [P, 16, EXPERTS], F32))

        const_in = sem("const_in_c")
        cleared = sem("cleared")
        table_out = sem("table_out")
        half_set = sem("half_set_c")
        masks_ok = sem("masks_ok")
        att_in = [sem("att_in0"), sem("att_in1")]
        emb_in = [sem(f"emb_in{i}") for i in range(CPB)]
        token_in = [sem(f"token_in{i}") for i in range(CPB)]
        bias_ok = sem("bias_ok")
        proj_ps = sem("proj_ps")
        resid_ok = sem("resid_ok")
        stats_raw = sem("stats_raw_c")
        stats_ok = sem("stats_ok_c")
        eps_ok = sem("eps_ok_c")
        rstd_ok = sem("rstd_ok_c")
        norm_ok = sem("norm_ok_c")
        base_ok = sem("base_ok")
        trans_ps = sem("trans_ps_c")
        trans_ok = sem("trans_ok_c")
        logits_ps = sem("logits_ps")
        top_ok = sem("top_ok")
        is_top_ok = sem("is_top_ok")
        below_ok = sem("below_ok")
        exp_ok = sem("exp_ok")
        marked_ok = sem("marked_ok")
        choice_ok = sem("choice_ok")
        onehot_ok = sem("onehot_ok")
        sum_ok = sem("sum_ok")
        gate_ok = sem("gate_ok")
        count_ps = sem("count_ps")
        carry_set = sem("carry_set")
        places_ok = sem("places_ok")
        carry_ok = sem("carry_ok")
        own_ok = sem("own_ok")
        place_ok = sem("place_ok")
        near_ok = sem("near_ok")
        over_ok = sem("over_ok")
        slot_ok = sem("slot_ok")
        scattered = [sem(f"scattered{i}") for i in range(CPB)]
        rows_out = [sem(f"rows_out{i}") for i in range(CPB)]

        def after(b, k, n=1):
            return b * (CPB * n) + (k + 1) * n

        def before(b, k, n=1):
            return b * (CPB * n) + k * n

        def slot_after(b, k, n):
            return b * (CPB // 2 * n) + (k // 2 + 1) * n

        def nxt(b, k, by=1):
            return (b, k + by) if k + by < CPB else (b + 1, k + by - CPB)

        def loops(eng, chunk):
            with eng.Fori(0, BATCH - 1) as b:
                for k in range(CPB):
                    chunk(b, k, False)
            for k in range(CPB):
                chunk(BATCH - 1, k, True)

        with nc.Block() as block:
            @block.sync
            def _(sp):
                def load_heads(b, k):
                    for d in range(KD):
                        att = dram["att"][bass.ds(b * HEADS + d * (HEADS // KD), HEADS // KD), 0:HD, k * CH:(k + 1) * CH]
                        sp.dma_start(att_t[:, k % 2, d], att).then_inc(att_in[k % 2], 16)

                def load_emb(b, k):
                    row = b * SEQ + k * CH
                    sp.dma_start(emb[:, k], dram["emb"][bass.ds(row, CH)].rearrange("(t p) n -> p t n", p=P)).then_inc(emb_in[k], 16)

                def load_tokens(b, k):
                    sp.dma_start(token_no[:, k], dram["tokens"][bass.ds(b * CPB + k, 1)].rearrange("a p t -> (a p) t")).then_inc(token_in[k], 16)

                for dst, src in ((ident, dram["ident"]), (tri_f, dram["tri"]), (b_o, dram["b_o"].to_broadcast([P, DM])),
                                 (w_o, dram["w_o"].rearrange("(k p) n -> p k n", p=P)),
                                 (w_router, dram["w_router"].rearrange("(k p) n -> p k n", p=P)),
                                 (expert_no, dram["expert_no"].rearrange("p (t e) -> p t e", e=EXPERTS))):
                    sp.dma_start(dst[:], src).then_inc(const_in, 16)
                def load_next_heads(b, k):
                    sp.wait_ge(proj_ps, after(b, k, 2))
                    load_heads(*nxt(b, k, 2))

                for k in range(2):
                    load_heads(0, k)
                for k in range(CPB):
                    load_emb(0, k)
                for k in range(3):
                    load_tokens(0, k)
                sp.wait_ge(cleared, 1)
                sp.dma_start(dram["slot_token"].rearrange("(p n) a -> p (n a)", p=P), no_token[:]).then_inc(table_out, 16)
                load_next_heads(0, 0)

                def chunk(b, k, last):
                    if not last:
                        sp.wait_ge(bias_ok, after(b, k))
                        load_emb(b + 1, k)
                    if not (last and k + 3 >= CPB):
                        load_next_heads(b, k + 1)
                    row = b * SEQ + k * CH
                    sp.wait_ge(base_ok, after(b, k))
                    sp.wait_ge(gate_ok, after(b, k))
                    sp.dma_start(dram["rows"][bass.ds(row, CH)].rearrange("(t p) n -> p t n", p=P), rows[:, k]).then_inc(rows_out[k], 16)
                    sp.dma_start(out[bass.ds(row, CH)].rearrange("(t p) n -> p t n", p=P), rows[:, k, :, DM:2 * DM]).then_inc(rows_out[k], 16)
                    if not (last and k + 3 >= CPB):
                        sp.wait_ge(scattered[(k - 1) % CPB], b * (16 * CT) + (16 * CT if k else 0))
                        load_tokens(*nxt(b, k, 3))
                    if last and k < EXPERT_RING:
                        experts.load(sp, dram, 0, k)

                loops(sp, chunk)
                for k in range(CPB):
                    sp.wait_ge(rows_out[k], BATCH * 32)
                    sp.wait_ge(scattered[k], BATCH * CT * 16)

            @block.gpsimd
            def _(pool):
                def add_bias(b, k):
                    pool.wait_ge(emb_in[k], b * 16 + 16)
                    pool.wait_ge(resid_ok, before(b, k, 2))
                    pool.tensor_tensor(emb_bias[:, k % 2], emb[:, k], b_o[:].rearrange("p (a n) -> p a n", a=1).to_broadcast([P, CT, DM]),
                                       ALU.add).then_inc(bias_ok, 1)

                def root(b, k):
                    pool.wait_ge(stats_ok, after(b, k, CT))
                    pool.tensor_tensor(var_eps[:, k % 2, :], mv[:, k % 2, :, 1], eps_sb[:], ALU.add).then_inc(eps_ok, 1)
                    pool.wait_ge(eps_ok, after(b, k))
                    pool.tensor_tensor(rstd[:, k % 2, :], var_eps[:, k % 2, :], neg_half[:], ALU.pow).then_inc(rstd_ok, 1)

                pool.memset(neg_half[:], -0.5).then_inc(half_set, 1)
                pool.memset(eps_sb[:], EPS).then_inc(half_set, 1)
                pool.memset(no_token[:], T).then_inc(cleared, 1)
                pool.memset(rows[:, :, :, 2 * DM:ROW], 0.0).then_inc(cleared, 1)
                pool.wait_ge(half_set, 2)
                pool.wait_ge(const_in, 16 * NCONST)
                add_bias(0, 0)
                root(0, 0)
                add_bias(0, 1)
                pool.wait_ge(table_out, 16)
                root(0, 1)
                add_bias(0, 2)

                def chunk(b, k, last):
                    pool.wait_ge(token_in[k], b * 16 + 16)
                    pool.wait_ge(slot_ok, after(b, k))
                    if not (last and k + 2 >= CPB):
                        root(*nxt(b, k, 2))
                    if not (last and k + 3 >= CPB):
                        add_bias(*nxt(b, k, 3))
                    for t in range(CT):
                        pool.indirect_dma_start(
                            dram["slot_token"], bass.IndirectOffsetOnAxis(ap=slot[:, k, t:t + 1], axis=0),
                            token_no[:, k, t:t + 1], None, bounds_check=SLOTS - 1, oob_is_err=False).then_inc(scattered[k], 16)

                loops(pool, chunk)

            @block.tensor
            def _(pe):
                def project(b, k):
                    pe.wait_ge(att_in[k % 2], slot_after(b, k, 32))
                    for t in range(CT):
                        if t % 2 == 0:
                            pe.wait_ge(resid_ok, before(b, k, 2))
                        for d in range(KD):
                            mm = pe.matmul(ps_p[:, t // 2, t % 2 * DM:(t % 2 + 1) * DM], att_t[:, k % 2, d, t * P:(t + 1) * P],
                                           w_o[:, d, :], start=d == 0, stop=d == KD - 1)
                        if t % 2:
                            mm.then_inc(proj_ps, 1)

                def transpose(b, k):
                    pe.wait_ge(norm_ok, after(b, k, CT))
                    pe.wait_ge(trans_ok, before(b, k))
                    for t in range(CT):
                        for d in range(KD):
                            mm = pe.transpose(ps_t[:, d, t * P:(t + 1) * P], rows[:, k, t, d * P:(d + 1) * P], ident[:])
                    mm.then_inc(trans_ps, 1)

                def logits(b, k):
                    pe.wait_ge(trans_ok, after(b, k))
                    pe.wait_ge(below_ok, before(b, k))
                    for t in range(CT):
                        for d in range(KD):
                            mm = pe.matmul(ps_l[:, t, :], rows_t[:, k % 2, d, t * P:(t + 1) * P], w_router[:, d, :],
                                           start=d == 0, stop=d == KD - 1)
                    mm.then_inc(logits_ps, 1)

                def count(b, k):
                    pe.wait_ge(onehot_ok, after(b, k))
                    pe.wait_ge(carry_ok, before(b, k))
                    for t in range(CT + 1):
                        for u in range(t):
                            mm = pe.matmul(ps_c[:, t, :], all_ones[:], onehot[:, k % 2, u, :], start=u == 0, stop=t == CT and u == CT - 1)
                        if t < CT:
                            pe.matmul(ps_c[:, t, :], earlier[:], onehot[:, k % 2, t, :], start=t == 0, stop=True)
                    mm.then_inc(count_ps, 1)

                pe.wait_ge(const_in, 16 * NCONST)
                project(0, 0)
                project(0, 1)
                transpose(0, 0)
                pe.wait_ge(masks_ok, 2)

                def chunk(b, k, last):
                    logits(b, k)
                    if not (last and k + 2 >= CPB):
                        project(*nxt(b, k, 2))
                    count(b, k)
                    if not (last and k == CPB - 1):
                        transpose(*nxt(b, k))

                loops(pe, chunk)

            @block.scalar
            def _(act):
                def copy_t(b, k):
                    act.wait_ge(trans_ps, after(b, k))
                    act.activation(rows_t[:, k % 2], ps_t[:], ACT.Copy).then_inc(trans_ok, 1)

                def chunk(b, k, last):
                    act.wait_ge(below_ok, after(b, k))
                    act.activation(expd[:, k % 2], below_top[:, k % 2], ACT.Exp).then_inc(exp_ok, 1)
                    if not (last and k == CPB - 1):
                        copy_t(*nxt(b, k))

                copy_t(0, 0)
                loops(act, chunk)

            @block.vector
            def _(dve):
                def wide(ap):
                    return ap.rearrange("p (t a) -> p t a", a=1).to_broadcast([P, CT, EXPERTS])

                def residual(b, k):
                    dve.wait_ge(bias_ok, after(b, k))
                    for h in range(2):
                        dve.wait_ge(proj_ps, after(b, k, 2) - (1 - h))
                        dve.tensor_tensor(resid[:, k % 2, 2 * h:2 * h + 2, :], ps_p[:, h, :].rearrange("p (t n) -> p t n", t=2),
                                          emb_bias[:, k % 2, 2 * h:2 * h + 2, :], ALU.add).then_inc(resid_ok, 1)

                def row_stats(b, k):
                    dve.wait_ge(resid_ok, after(b, k, 2))
                    for t in range(CT):
                        dve.bn_stats(stats[:, t, :], resid[:, k % 2, t, :]).then_inc(stats_raw, 1)

                def row_moments(b, k):
                    for t in range(CT):
                        dve.bn_aggr(mv[:, k % 2, t, :], stats[:, t, :]).then_inc(stats_ok, 1)

                def normalise(b, k):
                    dve.wait_ge(rstd_ok, after(b, k))
                    dve.wait_ge(rows_out[k], b * 32)
                    for t in range(CT):
                        dve.tensor_scalar(rows[:, k, t, 0:DM], resid[:, k % 2, t, :], mv[:, k % 2, t, 0:1], rstd[:, k % 2, t:t + 1],
                                          ALU.subtract, ALU.mult).then_inc(norm_ok, 1)

                def base(b, k):
                    dve.wait_ge(norm_ok, after(b, k, CT))
                    dve.tensor_tensor(rows[:, k, :, DM:2 * DM], resid[:, k % 2], rows[:, k, :, 0:DM], ALU.add).then_inc(base_ok, 1)

                def top_logit(b, k):
                    dve.wait_ge(logits_ps, after(b, k))
                    dve.tensor_reduce(top[:, k % 2], ps_l[:], AX.X, ALU.max).then_inc(top_ok, 1)

                def compare(b, k):
                    dve.wait_ge(top_ok, after(b, k))
                    dve.tensor_tensor(is_top[:, k % 2], ps_l[:], wide(top[:, k % 2]), ALU.is_equal).then_inc(is_top_ok, 1)
                    dve.tensor_tensor(below_top[:, k % 2], ps_l[:], wide(top[:, k % 2]), ALU.subtract).then_inc(below_ok, 1)

                def mark(b, k):
                    dve.wait_ge(is_top_ok, after(b, k))
                    dve.scalar_tensor_tensor(marked[:, k % 2], is_top[:, k % 2], -4.0 * EXPERTS, expert_no[:], ALU.mult, ALU.add).then_inc(marked_ok, 1)

                def choose(b, k):
                    dve.wait_ge(marked_ok, after(b, k))
                    dve.tensor_reduce(choice[:, k % 2], marked[:, k % 2], AX.X, ALU.min).then_inc(choice_ok, 1)

                def one_hot(b, k):
                    dve.wait_ge(choice_ok, after(b, k))
                    dve.tensor_tensor(onehot[:, k % 2], marked[:, k % 2], wide(choice[:, k % 2]), ALU.is_equal).then_inc(onehot_ok, 1)

                def gate(b, k):
                    dve.wait_ge(exp_ok, after(b, k))
                    dve.tensor_reduce(exp_sum[:, k % 2], expd[:, k % 2], AX.X, ALU.add).then_inc(sum_ok, 1)
                    dve.wait_ge(sum_ok, after(b, k))
                    dve.wait_ge(rows_out[k], b * 32)
                    dve.reciprocal(rows[:, k, :, 2 * DM:2 * DM + 1], exp_sum[:, k % 2].rearrange("p (t a) -> p t a", a=1)).then_inc(gate_ok, 1)

                def counts(b, k):
                    dve.wait_ge(count_ps, after(b, k))
                    old = carry[:, k % 2, :].rearrange("p (a e) -> p a e", a=1).to_broadcast([P, CT, EXPERTS])
                    dve.tensor_tensor(places[:, k % 2], ps_c[:, 0:CT, :], old, ALU.add).then_inc(places_ok, 1)
                    dve.tensor_tensor(carry[:, 1 - k % 2, :], ps_c[:, CT, :], carry[:, k % 2, :], ALU.add).then_inc(carry_ok, 1)

                def own(b, k):
                    dve.wait_ge(places_ok, after(b, k))
                    dve.tensor_tensor(own_place[:, k % 2], places[:, k % 2], onehot[:, k % 2], ALU.mult).then_inc(own_ok, 1)

                def slots(b, k):
                    dve.wait_ge(own_ok, after(b, k))
                    dve.tensor_reduce(place[:, k % 2], own_place[:, k % 2], AX.X, ALU.add).then_inc(place_ok, 1)
                    dve.wait_ge(place_ok, after(b, k))
                    dve.scalar_tensor_tensor(slot_near[:, k % 2], choice[:, k % 2], float(CAP), place[:, k % 2], ALU.mult, ALU.add).then_inc(near_ok, 1)
                    dve.tensor_scalar(over[:, k % 2], place[:, k % 2], float(CAP), FAR, ALU.is_ge, ALU.mult).then_inc(over_ok, 1)
                    dve.wait_ge(over_ok, after(b, k))
                    dve.wait_ge(scattered[k], b * (16 * CT))
                    dve.scalar_tensor_tensor(slot[:, k], slot_near[:, k % 2], 5.0 * EXPERTS * CAP, over[:, k % 2], ALU.add, ALU.add).then_inc(slot_ok, 1)

                dve.memset(all_ones[:], 1.0).then_inc(masks_ok, 1)
                dve.memset(carry[:], 0.0).then_inc(carry_set, 1)
                dve.wait_ge(const_in, 16 * NCONST)
                dve.tensor_copy(earlier[:], tri_f[:]).then_inc(masks_ok, 1)
                residual(0, 0)
                row_stats(0, 0)
                dve.wait_ge(stats_raw, CT)
                row_moments(0, 0)
                normalise(0, 0)
                base(0, 0)
                dve.wait_ge(carry_set, 1)
                dve.wait_ge(cleared, 2)

                def chunk(b, k, last):
                    more = not (last and k == CPB - 1)
                    n = nxt(b, k)
                    if more:
                        residual(*n)
                    top_logit(b, k)
                    if more:
                        row_stats(*n)
                    compare(b, k)
                    if more:
                        dve.wait_ge(stats_raw, after(*n, CT))
                    mark(b, k)
                    if more:
                        row_moments(*n)
                    choose(b, k)
                    one_hot(b, k)
                    gate(b, k)
                    if more:
                        normalise(*n)
                    counts(b, k)
                    if more:
                        base(*n)
                    own(b, k)
                    slots(b, k)

                loops(dve, chunk)


def phase_d(nc, dram, out, experts):
    PAIRS_E = EXPERTS // 2
    RING = EXPERT_RING
    STEPS = PAIRS_E // RING
    PS = 2 * CAP
    NB = PS // P
    HALF = P // 2
    assert PS % P == 0

    with ExitStack() as ctx:
        def sb(name, shape, dt=F32):
            return ctx.enter_context(nc.sbuf_tensor(name, shape, dt))

        sem = semaphores(nc, ctx)

        ident = sb("ident_d", [P, P])
        w_gate, w_up, w_down = experts.gate, experts.up, experts.down
        tokens = sb("tokens_d", [P, RING, NB], I32)
        rows = sb("rows_d", [P, RING, NB, ROW])
        rows_t = sb("rows_td", [P, 2, KD, PS])
        silu = sb("silu", [P, 2, 2, CAP])
        hidden = sb("hidden", [P, 2, 2, 2, CAP])
        result = sb("result", [P, 2, NB, DM])
        ps_t = [ctx.enter_context(nc.psum_tensor(f"ps_td{i}", [P, KD, 2 * P], F32)) for i in range(2)]
        ps_g = [ctx.enter_context(nc.psum_tensor(f"ps_g{i}", [P, CH], F32)) for i in range(2)]
        ps_u = [ctx.enter_context(nc.psum_tensor(f"ps_u{i}", [P, CH], F32)) for i in range(2)]
        ps_y = [ctx.enter_context(nc.psum_tensor(f"ps_y{i}", [P, CH], F32)) for i in range(2)]

        carrier = sb("carrier", [P, 1])

        const_in = sem("const_in_d")
        carried = sem("carried")
        rows_set = sem("rows_set")
        gate_up_in, down_in = experts.gate_up_in, experts.down_in
        tokens_in = [sem(f"tokens_in{i}") for i in range(RING)]
        rows_in = [sem(f"rows_in_d{i}") for i in range(RING)]
        trans_ps = sem("trans_ps_d")
        trans_ok = sem("trans_ok_d")
        gate_ps = sem("gate_ps")
        up_ps = sem("up_ps")
        silu_ok = sem("silu_ok")
        hidden_ok = sem("hidden_ok")
        down_ps = sem("down_ps")
        result_ok = [sem("result_ok0"), sem("result_ok1")]
        scattered = [sem("scattered_d0"), sem("scattered_d1")]

        NT = -(-NB // 2)

        def after(s, k, n=1):
            return s * (RING * n) + (k + 1) * n

        def before(s, k, n=1):
            return s * (RING * n) + k * n

        def nxt(s, k, by=1):
            return (s, k + by) if k + by < RING else (s + 1, k + by - RING)

        def loops(eng, pair):
            with eng.Fori(0, STEPS - 1) as s:
                for k in range(RING):
                    pair(s, k, False)
            for k in range(RING):
                pair(STEPS - 1, k, True)

        with nc.Block() as block:
            @block.sync
            def _(sp):
                def load_tokens(s, k):
                    src = dram["slot_token"][bass.ds(s * (RING * PS) + k * PS, PS)].rearrange("(p b) a -> p (b a)", b=NB)
                    sp.dma_start(tokens[:, k, :], src).then_inc(tokens_in[k], 16)

                for k in range(RING):
                    load_tokens(0, k)
                sp.dma_start(ident[:], dram["ident"]).then_inc(const_in, 16)
                def pair(s, k, last):
                    if last:
                        return
                    sp.wait_ge(down_ps, after(s, k, NB))
                    experts.load(sp, dram, s + 1, k)
                    sp.wait_ge(scattered[k % 2], s * (RING // 2 * NB * 16) + (k // 2 + 1) * NB * 16)
                    load_tokens(s + 1, k)

                loops(sp, pair)
                for i in range(2):
                    sp.wait_ge(scattered[i], PAIRS_E // 2 * NB * 16)

            @block.gpsimd
            def _(pool):
                def gather(s, k):
                    for i in range(NB):
                        pool.indirect_dma_start(rows[:, k, i, :], None, dram["rows"],
                                                bass.IndirectOffsetOnAxis(ap=tokens[:, k, i:i + 1], axis=0),
                                                bounds_check=T - 1, oob_is_err=False).then_inc(rows_in[k], 16)

                for k in range(3):
                    pool.wait_ge(rows_set, k + 1)
                    pool.wait_ge(tokens_in[k], 16)
                    gather(0, k)

                def pair(s, k, last):
                    for i in range(NB):
                        n = NB * k + i
                        pool.wait_ge(result_ok[n % 2], s * (RING * NB // 2) + n // 2 + 1)
                        if not last:
                            carry_wait(s, k, i)
                        pool.indirect_dma_start(out, bass.IndirectOffsetOnAxis(ap=tokens[:, k, i:i + 1], axis=0),
                                                result[:, k % 2, i, :], None,
                                                bounds_check=T - 1, oob_is_err=False).then_inc(scattered[k % 2], 16)
                    if not (last and k + 3 >= RING):
                        ahead = nxt(s, k, 3)
                        pool.wait_ge(tokens_in[ahead[1]], ahead[0] * 16 + 16)
                        if not last:
                            carry_wait(s, k, NB)
                        gather(*ahead)

                def carry_wait(s, k, n):
                    pool.wait_ge(carried, s * (RING * (NB + 1)) + k * (NB + 1) + n + 1)
                    pool.tensor_tensor(carrier[:], carrier[:], carrier[:], ALU.mult).then_inc(carried, 1)

                pool.memset(carrier[:], 0.0).then_inc(carried, 1)
                pool.wait_ge(carried, 1)
                pool.wait_ge(rows_set, RING)
                loops(pool, pair)

            @block.tensor
            def _(pe):
                def transpose(s, k):
                    pe.wait_ge(rows_in[k], s * (NB * 16) + NB * 16)
                    for i in range(NB):
                        b = NT * k + i // 2
                        if i % 2 == 0 and not (isinstance(s, int) and s == 0 and b < 2):
                            pe.wait_ge(trans_ok, s * (RING * NT) + b - 1)
                        for d in range(KD):
                            mm = pe.transpose(ps_t[b % 2][:, d, i % 2 * P:(i % 2 + 1) * P], rows[:, k, i, d * P:(d + 1) * P], ident[:])
                        if i % 2 or i == NB - 1:
                            mm.then_inc(trans_ps, 1)

                def gate_up(s, k, e):
                    for bank, w, done, free in ((ps_g, w_gate, gate_ps, silu_ok), (ps_u, w_up, up_ps, hidden_ok)):
                        for m in range(2):
                            pe.wait_ge(free, s * (4 * RING) + 4 * k + 2 * e)
                            for d in range(KD):
                                by_half = rows_t[:, k % 2, d, :].rearrange("p (b e c) -> p b e c", e=2, c=HALF)
                                mm = pe.matmul(bank[m][:, 0:CAP], w[:, k, KD * e + d, m * P:(m + 1) * P],
                                               by_half[:, :, e, :], start=d == 0, stop=d == KD - 1)
                            mm.then_inc(done, 1)

                def down(s, k, i):
                    n = NB * k + i
                    pe.wait_ge(result_ok[n % 2], s * (RING * NB // 2) + n // 2)
                    for e in range(2):
                        pe.wait_ge(hidden_ok, s * (4 * RING) + 4 * k + 2 * e + 2)
                        for f in range(FF // P):
                            mm = pe.matmul(ps_y[n % 2][e * HALF:(e + 1) * HALF, 0:DM], hidden[:, k % 2, e, f, i * HALF:(i + 1) * HALF],
                                           w_down[:, k, (FF // P) * e + f, :], start=f == 0, stop=f == FF // P - 1)
                    mm.then_inc(down_ps, 1)

                pe.wait_ge(const_in, 16)
                transpose(0, 0)

                def pair(s, k, last):
                    pe.wait_ge(gate_up_in[k], s * 64 + 64)
                    pe.wait_ge(trans_ok, after(s, k, NT))
                    gate_up(s, k, 0)
                    if not (last and k == RING - 1):
                        transpose(*nxt(s, k))
                    gate_up(s, k, 1)
                    pe.wait_ge(down_in[k], s * 32 + 32)
                    for i in range(NB):
                        down(s, k, i)

                loops(pe, pair)

            @block.scalar
            def _(act):
                def copy_t(s, k):
                    for i in range(NT):
                        b = NT * k + i
                        cols = min(2 * P, PS - 2 * P * i)
                        act.wait_ge(trans_ps, s * (RING * NT) + b + 1)
                        act.activation(rows_t[:, k % 2, :, 2 * P * i:2 * P * i + cols], ps_t[b % 2][:, :, 0:cols], ACT.Copy).then_inc(trans_ok, 1)

                def silus(s, k, e):
                    for m in range(2):
                        act.wait_ge(gate_ps, s * (4 * RING) + 4 * k + 2 * e + m + 1)
                        act.wait_ge(hidden_ok, s * (4 * RING) + 4 * k + 2 * e)
                        act.activation(silu[:, e, m, :], ps_g[m][:, 0:CAP], ACT.Silu).then_inc(silu_ok, 1)

                def pair(s, k, last):
                    silus(s, k, 0)
                    if not (last and k == RING - 1):
                        copy_t(*nxt(s, k))
                    silus(s, k, 1)

                copy_t(0, 0)
                loops(act, pair)

            @block.vector
            def _(dve):
                for k in range(RING):
                    dve.memset(rows[:, k], 0.0).then_inc(rows_set, 1)

                def multiply(s, k, e):
                    for m in range(2):
                        dve.wait_ge(silu_ok, s * (4 * RING) + 4 * k + 2 * e + m + 1)
                        dve.wait_ge(up_ps, s * (4 * RING) + 4 * k + 2 * e + m + 1)
                        dve.tensor_tensor(hidden[:, k % 2, e, m, :], ps_u[m][:, 0:CAP], silu[:, e, m, :], ALU.mult).then_inc(hidden_ok, 1)

                def add(s, k, i):
                    n = NB * k + i
                    dve.wait_ge(down_ps, s * (RING * NB) + n + 1)
                    dve.wait_ge(scattered[k % 2], s * (RING // 2 * NB * 16) + (k // 2) * NB * 16)
                    dve.scalar_tensor_tensor(result[:, k % 2, i, :], ps_y[n % 2][:, 0:DM], rows[:, k, i, 2 * DM:2 * DM + 1],
                                             rows[:, k, i, DM:2 * DM], ALU.mult, ALU.add).then_inc(result_ok[n % 2], 1)

                def pair(s, k, last):
                    multiply(s, k, 0)
                    multiply(s, k, 1)
                    for i in range(NB):
                        add(s, k, i)

                loops(dve, pair)


def build(nc, dram, out, phases="ABCD"):
    if "A" in phases:
        phase_a(nc, dram, out)
    if "B" in phases:
        phase_b(nc, dram, out)
    with ExitStack() as ctx:
        if "C" in phases:
            experts = ExpertWeights(nc, ctx)
            phase_c(nc, dram, out, experts)
        if "D" in phases:
            phase_d(nc, dram, out, experts)


def tables():
    pos = np.arange(SEQ, dtype=np.float32)[:, None]
    pair = np.arange(DM // 2, dtype=np.float32)
    theta = (np.float32(ROPE_BASE) ** (np.float32(-2.0) * pair) / np.float32(DM // 2)).astype(np.float32)
    angle = (pos * theta[None, :]).astype(np.float32).T
    return np.ascontiguousarray(np.cos(angle)), np.ascontiguousarray(np.sin(angle))


def laid_out(inputs):
    f = lambda name: np.asarray(inputs[name])
    a = lambda name: np.asarray(inputs["L0_attn_" + name])
    pairs = lambda w: np.concatenate([w[..., 0::2], w[..., 1::2]], axis=-1)
    cos, sin = tables()
    cols = [a("Wd_q_b"), a("Wd_kv_b")]
    for name in ("Wq_r_b", "Wu_q_b", "Wk_r_b", "Wu_k_b"):
        cols += [a(name)[0::2], a(name)[1::2]]
    tri = np.triu(np.ones((P, P), np.float32), 1)
    out = {
        "ids": np.asarray(inputs["x"]).astype(np.int32).reshape(NCH, CT, P).transpose(0, 2, 1),
        "table": f("L0_tok_weight"), "ident": np.eye(P, dtype=np.float32), "tri": tri, "cos": cos, "sin": sin,
        "w_dq": a("Wd_q_w"), "w_dkv": a("Wd_kv_w"), "w_uq": pairs(a("Wu_q_w")), "w_qr": pairs(a("Wq_r_w")),
        "w_uk": pairs(a("Wu_k_w")), "w_kr": pairs(a("Wk_r_w")), "w_uv": a("Wu_v_w"), "w_o": a("Wo_w"),
        "b_cols": np.stack(cols, axis=1), "b_v": a("Wu_v_b")[None], "b_o": a("Wo_b")[None],
        "w_router": f("L0_ffn_w_router"), "w_gate": f("L0_ffn_w_gate"), "w_up": f("L0_ffn_w_up"), "w_down": f("L0_ffn_w_down"),
        "expert_no": np.tile(np.arange(EXPERTS, dtype=np.float32) - EXPERTS, (P, CT)),
        "tokens": np.arange(T, dtype=np.int32).reshape(NCH, CT, P).transpose(0, 2, 1),
    }
    return {k: np.ascontiguousarray(v) for k, v in out.items()}


def program(nc, arrays, phases="ABCD"):
    dram = {}
    for name, array in arrays.items():
        dt = I32 if array.dtype == np.int32 else F32
        dram[name] = nc.dram_tensor(f"in_{name}", array.shape, dt, kind="ExternalInput").ap()
    dram["qk"] = [nc.dram_tensor(f"split_{x}", (BATCH * HEADS, PARTS, 2, HD // 2, SEQ), BF16, kind="Internal").ap() for x in "qk"]
    dram["vext"] = nc.dram_tensor("vext", (QUADS, SEQ, QUAD * VW), F32, kind="Internal").ap()
    dram["emb"] = nc.dram_tensor("emb_rows", (T, DM), F32, kind="Internal").ap()
    dram["att"] = nc.dram_tensor("att", (BATCH * HEADS, VW, SEQ), F32, kind="Internal").ap()
    dram["recip"] = nc.dram_tensor("recip_rows_dram", (2, QUAD, CH), F32, kind="Internal").ap()
    dram["rows"] = nc.dram_tensor("rows", (T, ROW), F32, kind="Internal").ap()
    dram["slot_token"] = nc.dram_tensor("slot_token", (SLOTS, 1), I32, kind="Internal").ap()
    out = nc.dram_tensor("out", (T, DM), F32, kind="ExternalOutput").ap()
    nc.disable_value_cache = True
    build(nc, dram, out, phases)


def kernel(**inputs):
    import concourse.bacc as bacc
    from concourse.bass_utils import run_bass_kernel_spmd

    arrays = laid_out(inputs)
    nc = bacc.Bacc("TRN2", target_bir_lowering=False, num_devices=1)
    program(nc, arrays)
    r = run_bass_kernel_spmd(nc, [{f"in_{k}": v for k, v in arrays.items()}], core_ids=[0])
    return r.results[0]["out"].reshape(BATCH, SEQ, DM)
```
